# Optimizing a Trainium2 kernel written in Bass

```python
import numpy as np
import jax
import jax.numpy as jnp

def _softmax(x, axis=-1):
    return jax.nn.softmax(x, axis=axis)

def _gelu(x):
    return jax.nn.gelu(x, approximate=True)

def _silu(x):
    return jax.nn.silu(x)

def _sigmoid(x):
    return jax.nn.sigmoid(x)

def _layernorm(x, axis=-1, eps=1e-05):
    m = jnp.mean(x, axis=axis, keepdims=True)
    v = jnp.var(x, axis=axis, keepdims=True)
    return (x - m) / jnp.sqrt(v + eps)

def _scatter_add(tgt, idx, src, axis=0):
    return tgt.at[idx].add(src)

def _segment_sum(src, seg, n):
    return jax.ops.segment_sum(src, seg, n)
kernel_name = 'mk_adj_resnorm_d1_adj_r2_dd10dc'

def setup_inputs(seed: int=0):
    np.random.seed(seed)
    _w = jnp.asarray

    def _rec_inputs():
        import jax
        import jax.numpy as jnp
        _gk = jax.random.key(seed)
        x = -0.0005207 + 1.001 * jax.random.normal(jax.random.fold_in(_gk, 1), (8192, 128), jnp.float32)
        _w = (1.0 + jnp.arange(8192, dtype=jnp.float32)) ** (-0.5)
        _w = _w / _w.mean()
        _pij = jnp.clip(0.00195312 * _w[:, None] * _w[None, :], 0.0, 1.0)
        _a = jax.random.uniform(jax.random.fold_in(_gk, 2), (8192, 8192)) < _pij
        _a = jnp.logical_or(_a, jnp.eye(8192, dtype=bool))
        _af = _a.astype(jnp.float32)
        _af = _af * jax.random.uniform(jax.random.fold_in(_gk, 3), (8192, 8192), jnp.float32, 0.05, 1)
        adj = _af
        return (x, adj)
    x, adj = _rec_inputs()

    def _L0_gnn_setup():
        import jax, jax.numpy as jnp
        import numpy as np
        ALPHA = 0.1
        N, F = (8192, 128)
        key = jax.random.key(seed)
        k1, k2, k3 = jax.random.split(key, 3)
        x = jax.random.normal(k1, (N, F), dtype=jnp.float32)
        adj = jax.random.uniform(k2, (N, N), dtype=jnp.float32)
        h = jax.random.normal(k3, (N, F), dtype=jnp.float32)
        return {'x': x, 'adj': adj, 'h': h}
    _L0_gnn_all = _L0_gnn_setup()
    _L0_gnn_in = {k: v for k, v in _L0_gnn_all.items() if k in ('h',)}
    del _L0_gnn_all
    return {'x': x, 'adj': adj, 'L0_gnn_h': _L0_gnn_in['h']}

def reference(x, adj, L0_gnn_h):
    import jax
    import jax.numpy as jnp

    def _L0_gnn_ref(x, adj, h):
        import jax, jax.numpy as jnp
        import numpy as np
        ALPHA = 0.1
        N, F = (8192, 128)
        return (1.0 - ALPHA) * (adj @ x) + ALPHA * h
    x = _layernorm(x + _L0_gnn_ref(x, adj, L0_gnn_h), axis=-1)
    return x

_drawn_inputs = setup_inputs


def setup_inputs(seed=0):
    import zlib

    import numpy as np

    out = dict(_drawn_inputs(seed))
    spreads = {}
    factors = {}
    for name, (base, spread) in spreads.items():
        noise = np.random.default_rng([zlib.crc32(name.encode()), seed]).standard_normal(out[name].shape)
        drawn = base * np.exp(spread * noise) if base else spread * noise
        out[name] = jnp.asarray(drawn.astype(out[name].dtype))
    for name, factor in factors.items():
        out[name] = (out[name] * factor).astype(out[name].dtype)
    return out
```

```python
from contextlib import ExitStack

import numpy as np

import concourse.bass as bass
from concourse import mybir
from concourse.alu_op_type import AluOpType as ALU

P = 128
N = 8192
F = 128
C = 4
W = C * P
G = N // W
TILE = C * W
TILES = G
HALF = TILES // 2
X_TILES = N // P * F // TILE
LEAD_IN = [("x", 0), *(("adj", s) for s in range(4)), ("x", 1), *(("adj", s) for s in range(4, HALF)),
           ("x", 2), ("x", 3)]
RAW, HEADS, RESTS = 8, 4, 4
ALPHA = 0.1
EPS = 1e-5


def build(nc, x, adj, h, out):
    fp32, fp32r = mybir.dt.float32, mybir.dt.float32r
    ACT = mybir.ActivationFunctionType

    with ExitStack() as ctx:
        def sbuf(name, shape, dtype=fp32):
            return ctx.enter_context(nc.sbuf_tensor(name, shape, dtype))

        def psum(name):
            return ctx.enter_context(nc.psum_tensor(name, [P, W], fp32))

        def sem(name):
            return ctx.enter_context(nc.semaphore(name))

        raw = sbuf("raw", [P, RAW, TILE])
        head = sbuf("head", [P, HEADS, TILE], fp32r)
        rest = sbuf("rest", [P, RESTS, TILE], fp32r)
        x_head = sbuf("x_head", [P, X_TILES * TILE], fp32r)
        x_rest = sbuf("x_rest", [P, X_TILES * TILE], fp32r)
        identity = sbuf("identity", [P, P])
        h_in = sbuf("h_in", [P, W])
        x_rows = sbuf("x_rows", [P, W])
        residual = sbuf("residual", [P, W])
        first_sum = sbuf("first_sum", [P, W])
        y_t = sbuf("y_t", [P, W])
        z = sbuf("z", [P, C, F])
        normed = sbuf("normed", [P, C, F])
        stats = sbuf("stats", [P, C, 6])
        mean_var = sbuf("mean_var", [P, C, 2])
        eps = sbuf("eps", [P, 1])
        std = sbuf("std", [P, C])
        rstd = sbuf("rstd", [P, C])

        acc = [psum("acc_first"), psum("acc_second")]
        turned = psum("turned")

        raw_landed = [sem(f"raw_landed_{i}") for i in range(RAW)]
        head_ready = sem("head_ready")
        rest_ready = sem("rest_ready")
        tile_used = sem("tile_used")
        first_saved = sem("first_saved")
        y_t_ready = sem("y_t_ready")
        turned_ready = sem("turned_ready")
        h_landed = sem("h_landed")
        h_scaled = sem("h_scaled")
        x_rows_ready = sem("x_rows_ready")
        residual_ready = sem("residual_ready")
        z_ready = sem("z_ready")
        stats_ready = sem("stats_ready")
        var_ready = sem("var_ready")
        std_ready = sem("std_ready")
        rstd_ready = sem("rstd_ready")
        normed_ready = sem("normed_ready")
        normed_free = sem("normed_free")
        zeroed = sem("zeroed")
        identity_ready = sem("identity_ready")
        eps_ready = sem("eps_ready")

        block = ctx.enter_context(nc.Block())

        def slot(s):
            return (s + X_TILES) % RAW

        def landings(g, s):
            return 16 * (TILES // RAW * g + (s + X_TILES) // RAW + 1)

        @block.sync
        def _(sp):
            def load(g, s):
                sp.wait_ge(rest_ready, TILES * g + (s + X_TILES - RAW + 1))
                sp.dma_start(raw[:, slot(s), :], adj[TILES * g + s]).then_inc(raw_landed[slot(s)], 16)

            for q, (what, i) in enumerate(LEAD_IN):
                if q >= RAW:
                    sp.wait_ge(rest_ready, q - RAW + 1)
                source = x[:, i * TILE:(i + 1) * TILE] if what == "x" else adj[i]
                sp.dma_start(raw[:, q % RAW, :], source).then_inc(raw_landed[q % RAW], 16)
            sp.dma_start(h_in[:, :], h[0]).then_inc(h_landed, 16)
            with sp.Fori(0, G - 1) as g:
                for s in range(HALF, HALF + TILES):
                    load(g, s)
                    if s == TILES:
                        sp.wait_ge(h_scaled, g + 1)
                        sp.dma_start(h_in[:, :], h[g + 1]).then_inc(h_landed, 16)
            for s in range(HALF, TILES):
                load(G - 1, s)

        @block.gpsimd
        def _(pool):
            nc.gpsimd.memset(eps[:, :], EPS).then_inc(eps_ready, 1)
            nc.gpsimd.memset(identity[:, :], 0.0).then_inc(zeroed, 1)
            pool.wait_ge(zeroed, 1)
            nc.gpsimd.affine_select(out=identity[:, :], in_=identity[:, :], compare_op=ALU.not_equal,
                                    fill=1.0, base=0, pattern=[[-1, P]],
                                    channel_multiplier=1).then_inc(identity_ready, 1)

            def make_residual(g):
                pool.wait_ge(h_landed, 16 * g + 16)
                nc.gpsimd.tensor_tensor(x_rows[:, :], x_head[:, bass.ds(g * W, W)].bitcast(fp32),
                                        x_rest[:, bass.ds(g * W, W)].bitcast(fp32),
                                        ALU.add).then_inc(x_rows_ready, 1)
                nc.gpsimd.tensor_scalar(residual[:, :], h_in[:, :], ALPHA, None,
                                        ALU.mult).then_inc(h_scaled, 1)
                pool.wait_ge(h_scaled, g + 1)
                pool.wait_ge(x_rows_ready, g + 1)
                nc.gpsimd.tensor_tensor(residual[:, :], residual[:, :], x_rows[:, :],
                                        ALU.add).then_inc(residual_ready, 1)

            pool.wait_ge(head_ready, len(LEAD_IN))
            pool.wait_ge(rest_ready, len(LEAD_IN))
            make_residual(0)
            with pool.Fori(1, G) as g:
                pool.wait_ge(z_ready, g)
                make_residual(g)

        @block.scalar
        def _(act):
            def make_head(g, s):
                act.wait_ge(raw_landed[slot(s)], landings(g, s))
                act.wait_ge(tile_used, TILES * g + (s - HEADS + 1))
                nc.scalar.copy(head[:, s % HEADS, :], raw[:, slot(s), :]).then_inc(head_ready, 1)

            def save_first(g):
                act.wait_ge(tile_used, TILES * g + HALF)
                nc.scalar.copy(first_sum[:, :], acc[0][:, :]).then_inc(first_saved, 1)

            def make_std(g):
                act.wait_ge(var_ready, g + 1)
                nc.scalar.activation(std[:, :], mean_var[:, :, 1], ACT.Sqrt,
                                     bias=eps[:, :]).then_inc(std_ready, 1)

            def store(g):
                act.wait_ge(normed_ready, g + 1)
                act.dma_start(out[g], normed[:, :, :]).then_inc(normed_free, 16)

            act.sem_inc(normed_free, 16)
            for q, (what, i) in enumerate(LEAD_IN):
                act.wait_ge(raw_landed[q % RAW], 16 * (q // RAW + 1))
                if what == "x":
                    target = x_head[:, i * TILE:(i + 1) * TILE]
                else:
                    target = head[:, i % HEADS, :]
                    if i >= HEADS:
                        act.wait_ge(tile_used, i - HEADS + 1)
                nc.scalar.copy(target, raw[:, q % RAW, :]).then_inc(head_ready, 1)
            act.wait_ge(eps_ready, 1)
            with act.Fori(0, G - 1) as g:
                for s in range(HALF, HALF + TILES):
                    if s == HALF + 3:
                        save_first(g)
                    if s == TILES + 6:
                        make_std(g)
                    make_head(g, s)
                store(g)
            for s in range(HALF, TILES):
                if s == HALF + 3:
                    save_first(G - 1)
                make_head(G - 1, s)
            make_std(G - 1)
            store(G - 1)
            act.wait_ge(normed_free, 16 * G + 16)

        @block.vector
        def _(dve):
            def make_rest(g, s):
                dve.wait_ge(raw_landed[slot(s)], landings(g, s))
                dve.wait_ge(head_ready, TILES * g + (X_TILES + s + 1))
                dve.wait_ge(tile_used, TILES * g + (s - RESTS + 1))
                nc.vector.tensor_tensor(rest[:, s % RESTS, :], raw[:, slot(s), :],
                                        head[:, s % HEADS, :].bitcast(fp32),
                                        ALU.subtract).then_inc(rest_ready, 1)

            def make_y_t(g):
                dve.wait_ge(tile_used, TILES * g + TILES)
                dve.wait_ge(first_saved, g + 1)
                nc.vector.tensor_tensor(y_t[:, :], acc[1][:, :], first_sum[:, :],
                                        ALU.add).then_inc(y_t_ready, 1)

            def make_z(g):
                dve.wait_ge(turned_ready, g + 1)
                dve.wait_ge(residual_ready, g + 1)
                nc.vector.scalar_tensor_tensor(out=z[:, :, :].rearrange("p c f -> p (c f)"),
                                               in0=turned[:, :], scalar=1.0 - ALPHA,
                                               in1=residual[:, :], op0=ALU.mult,
                                               op1=ALU.add).then_inc(z_ready, 1)

            def make_stats(g):
                dve.wait_ge(z_ready, g + 1)
                for c in range(C):
                    nc.vector.bn_stats(stats[:, c, :], z[:, c, :]).then_inc(stats_ready, 1)

            def make_var(g):
                for c in range(C):
                    last = nc.vector.bn_aggr(mean_var[:, c, :], stats[:, c, :])
                last.then_inc(var_ready, 1)

            def make_normed(g):
                dve.wait_ge(std_ready, g + 1)
                nc.vector.reciprocal(rstd[:, :], std[:, :]).then_inc(rstd_ready, 1)
                dve.wait_ge(rstd_ready, g + 1)
                dve.wait_ge(normed_free, 16 * g + 16)
                for c in range(C):
                    last = nc.vector.tensor_scalar(normed[:, c, :], z[:, c, :], mean_var[:, c, 0:1],
                                                   rstd[:, c:c + 1], ALU.subtract, ALU.mult)
                last.then_inc(normed_ready, 1)

            for q, (what, i) in enumerate(LEAD_IN):
                dve.wait_ge(raw_landed[q % RAW], 16 * (q // RAW + 1))
                dve.wait_ge(head_ready, q + 1)
                if what == "x":
                    part = slice(i * TILE, (i + 1) * TILE)
                    target, its_head = x_rest[:, part], x_head[:, part]
                else:
                    target, its_head = rest[:, i % RESTS, :], head[:, i % HEADS, :]
                    if i >= RESTS:
                        dve.wait_ge(tile_used, i - RESTS + 1)
                nc.vector.tensor_tensor(target, raw[:, q % RAW, :], its_head.bitcast(fp32),
                                        ALU.subtract).then_inc(rest_ready, 1)
            with dve.Fori(0, G - 1) as g:
                for s in range(HALF, HALF + TILES):
                    if s == TILES + 1:
                        make_y_t(g)
                    if s == TILES + 3:
                        make_z(g)
                    if s == TILES + 4:
                        make_stats(g)
                        dve.wait_ge(stats_ready, C * g + C)
                    if s == TILES + 6:
                        make_normed(g)
                    make_rest(g, s)
                    if s == TILES + 4:
                        make_var(g)
            for s in range(HALF, TILES):
                make_rest(G - 1, s)
            make_y_t(G - 1)
            make_z(G - 1)
            make_stats(G - 1)
            dve.wait_ge(stats_ready, C * G)
            make_var(G - 1)
            make_normed(G - 1)

        @block.tensor
        def _(pe):
            def multiply(g, s, ready):
                bank = acc[s // HALF % 2]
                place = s % HALF
                blocks = [slice(j * F, (j + 1) * F) for j in range(C * (s % TILES), C * (s % TILES) + C)]
                pe.wait_ge(head_ready, ready)
                for j, k in enumerate(blocks):
                    moving = head[:, s % HEADS, j * W:(j + 1) * W]
                    nc.tensor.matmul(bank[:, :], x_head[:, k], moving,
                                     start=(place == 0 and j == 0), stop=False)
                    nc.tensor.matmul(bank[:, :], x_rest[:, k], moving, start=False, stop=False)
                pe.wait_ge(rest_ready, ready)
                for j, k in enumerate(blocks):
                    last = nc.tensor.matmul(bank[:, :], x_head[:, k], rest[:, s % RESTS, j * W:(j + 1) * W],
                                            start=False, stop=(place == HALF - 1 and j == C - 1))
                last.then_inc(tile_used, 1)

            def turn(g):
                pe.wait_ge(y_t_ready, g + 1)
                for c in range(C):
                    last = nc.tensor.transpose(turned[:, c * P:(c + 1) * P], y_t[:, c * P:(c + 1) * P],
                                               identity[:, :])
                last.then_inc(turned_ready, 1)

            pe.wait_ge(identity_ready, 1)
            for q, (what, i) in enumerate(LEAD_IN):
                if what == "x":
                    pe.wait_ge(head_ready, q + 1)
                    pe.wait_ge(rest_ready, q + 1)
                else:
                    multiply(0, i, q + 1)
            with pe.Fori(0, G - 1) as g:
                for s in range(HALF, HALF + TILES):
                    if s == TILES:
                        pe.wait_ge(first_saved, g + 1)
                    if s == TILES + 2:
                        turn(g)
                    multiply(g, s, TILES * g + (X_TILES + s + 1))
            for s in range(HALF, TILES):
                multiply(G - 1, s, TILES * (G - 1) + X_TILES + s + 1)
            turn(G - 1)


def kernel(x, adj, L0_gnn_h):
    import concourse.bacc as bacc
    from concourse.bass_utils import run_bass_kernel_spmd

    x, adj, h = (np.asarray(a) for a in (x, adj, L0_gnn_h))
    arrays = {
        "x": np.ascontiguousarray(x.reshape(G, P, C * F).transpose(1, 0, 2).reshape(P, -1)),
        "adj": np.ascontiguousarray(
            adj.reshape(G, P, C, G, P, C).transpose(0, 3, 4, 5, 2, 1).reshape(G * TILES, P, TILE)),
        "h": np.ascontiguousarray(h.reshape(G, P, C * F)),
    }
    nc = bacc.Bacc("TRN2", target_bir_lowering=False, num_devices=1)
    fp32 = mybir.dt.float32
    args = [nc.dram_tensor(name, a.shape, fp32, kind="ExternalInput").ap() for name, a in arrays.items()]
    out = nc.dram_tensor("out", (G, P, C * F), fp32, kind="ExternalOutput").ap()
    build(nc, *args, out)
    result = run_bass_kernel_spmd(nc, [arrays], core_ids=[0]).results[0]["out"]
    return result.reshape(N, F)
```

```python
from contextlib import ExitStack

import numpy as np

import concourse.bass as bass
from concourse import mybir
from concourse.alu_op_type import AluOpType as ALU

P = 128
N = 8192
F = 128
C = 4
W = C * P
G = N // W
TILE = C * W
TILES = N // (C * P)
HALF = TILES // 2
X_TILES = N // P * F // TILE
PER_X = TILES // X_TILES
LEAD_IN = [("x", 0), *(("adj", s) for s in range(PER_X)), ("x", 1), *(("adj", s) for s in range(PER_X, HALF)),
           ("x", 2), ("x", 3)]
RAW, HEADS, RESTS = 8, 4, 4
PIECES = [(s, j, blocks) for s in range(HALF, TILES) for blocks in [C // 4 if s == TILES - 1 else C // 2]
          for j in range(0, C, blocks)]
SPLITS = TILES * (G - 1) + X_TILES + HALF
ALPHA = 0.1
EPS = 1e-5


def build(nc, x, adj, h, out):
    fp32, fp32r = mybir.dt.float32, mybir.dt.float32r
    ACT = mybir.ActivationFunctionType

    with ExitStack() as ctx:
        def sbuf(name, shape, dtype=fp32):
            return ctx.enter_context(nc.sbuf_tensor(name, shape, dtype))

        def psum(name):
            return ctx.enter_context(nc.psum_tensor(name, [P, W], fp32))

        def sem(name):
            return ctx.enter_context(nc.semaphore(name))

        raw = sbuf("raw", [P, RAW, TILE])
        head = sbuf("head", [P, HEADS, TILE], fp32r)
        rest = sbuf("rest", [P, RESTS, TILE], fp32r)
        x_head = sbuf("x_head", [P, X_TILES * TILE], fp32r)
        x_rest = sbuf("x_rest", [P, X_TILES * TILE], fp32r)
        identity = sbuf("identity", [P, P])
        h_in = sbuf("h_in", [P, W])
        residual = sbuf("residual", [P, W])
        first_sum = sbuf("first_sum", [P, W])
        y_t = sbuf("y_t", [P, W])
        z = sbuf("z", [P, C, F])
        normed = sbuf("normed", [P, C, F])
        stats = sbuf("stats", [P, C, 6])
        mean_var = sbuf("mean_var", [P, C, 2])
        eps_quarter = sbuf("eps_quarter", [P, 1])
        half_std = sbuf("half_std", [P, C])
        inverse = sbuf("inverse", [P, C])
        ratio = sbuf("ratio", [P, C])
        std = sbuf("std", [P, C])
        rstd = sbuf("rstd", [P, C])

        acc = [psum("acc_first"), psum("acc_second")]
        turned = psum("turned")
        last_turned = [psum(f"last_turned_{i}") for i in range(2)]

        raw_landed = [sem(f"raw_landed_{i}") for i in range(RAW)]
        piece_landed = [sem(f"piece_landed_{i}") for i in range(len(PIECES))]
        head_ready = sem("head_ready")
        rest_ready = sem("rest_ready")
        tile_used = sem("tile_used")
        first_saved = sem("first_saved")
        y_t_ready = sem("y_t_ready")
        turned_ready = sem("turned_ready")
        h_landed = sem("h_landed")
        x_rows_ready = sem("x_rows_ready")
        residual_ready = sem("residual_ready")
        z_ready = sem("z_ready")
        stats_ready = sem("stats_ready")
        var_ready = sem("var_ready")
        half_std_ready = sem("half_std_ready")
        std_steps = sem("std_steps")
        rstd_ready = sem("rstd_ready")
        normed_ready = sem("normed_ready")
        normed_free = sem("normed_free")
        last_y_ready = sem("last_y_ready")
        last_turned_ready = sem("last_turned_ready")
        last_z_ready = sem("last_z_ready")
        zeroed = sem("zeroed")
        identity_ready = sem("identity_ready")
        eps_ready = sem("eps_ready")

        block = ctx.enter_context(nc.Block())

        def slot(s):
            return (s + X_TILES) % RAW

        def landings(g, s):
            return 16 * (TILES // RAW * g + (s + X_TILES) // RAW + 1)

        @block.sync
        def _(sp):
            def load(g, s):
                sp.wait_ge(rest_ready, TILES * g + (s + X_TILES - RAW + 1))
                sp.dma_start(raw[:, slot(s), :], adj[TILES * g + s]).then_inc(raw_landed[slot(s)], 16)

            for q, (what, i) in enumerate(LEAD_IN):
                if q >= RAW:
                    sp.wait_ge(rest_ready, q - RAW + 1)
                source = x[:, i * TILE:(i + 1) * TILE] if what == "x" else adj[i]
                sp.dma_start(raw[:, q % RAW, :], source).then_inc(raw_landed[q % RAW], 16)
            sp.dma_start(h_in[:, :], h[0]).then_inc(h_landed, 16)
            with sp.Fori(0, G - 1) as g:
                for s in range(HALF, HALF + TILES):
                    load(g, s)
                    if s == TILES:
                        sp.wait_ge(residual_ready, g + 1)
                        sp.dma_start(h_in[:, :], h[g + 1]).then_inc(h_landed, 16)
            for n, (s, j, blocks) in enumerate(PIECES):
                part = slice(j * W, (j + blocks) * W)
                sp.wait_ge(rest_ready, TILES * (G - 1) + s + X_TILES - RAW + 1)
                sp.dma_start(raw[:, slot(s), part], adj[TILES * (G - 1) + s][:, part]).then_inc(piece_landed[n], 16)
            for part in range(2):
                sp.wait_ge(normed_ready, G + part)
                blocks = slice(part * C // 2, (part + 1) * C // 2)
                sp.dma_start(out[G - 1][:, part * W // 2:(part + 1) * W // 2],
                             normed[:, blocks, :]).then_inc(normed_free, 16)
            sp.wait_ge(normed_free, 16 * (G + 2))

        @block.gpsimd
        def _(pool):
            nc.gpsimd.memset(eps_quarter[:, :], EPS / 4).then_inc(eps_ready, 1)
            nc.gpsimd.memset(identity[:, :], 0.0).then_inc(zeroed, 1)
            pool.wait_ge(zeroed, 1)
            nc.gpsimd.affine_select(out=identity[:, :], in_=identity[:, :], compare_op=ALU.not_equal,
                                    fill=1.0, base=0, pattern=[[-1, P]],
                                    channel_multiplier=1).then_inc(identity_ready, 1)

        @block.scalar
        def _(act):
            def make_head(g, s):
                act.wait_ge(raw_landed[slot(s)], landings(g, s))
                act.wait_ge(tile_used, TILES * g + (s - HEADS + 1))
                nc.scalar.copy(head[:, s % HEADS, :], raw[:, slot(s), :]).then_inc(head_ready, 1)

            def save_first(g):
                act.wait_ge(tile_used, TILES * g + HALF)
                nc.scalar.copy(first_sum[:, :], acc[0][:, :]).then_inc(first_saved, 1)

            def make_half_std(g):
                act.wait_ge(var_ready, g + 1)
                nc.scalar.activation(half_std[:, :], mean_var[:, :, 1], ACT.Sqrt, scale=0.25,
                                     bias=eps_quarter[:, :]).then_inc(half_std_ready, 1)

            def store(g):
                act.wait_ge(normed_ready, g + 1)
                act.dma_start(out[g], normed[:, :, :]).then_inc(normed_free, 16)

            act.sem_inc(normed_free, 16)
            for q, (what, i) in enumerate(LEAD_IN):
                act.wait_ge(raw_landed[q % RAW], 16 * (q // RAW + 1))
                if what == "x":
                    target = x_head[:, i * TILE:(i + 1) * TILE]
                else:
                    target = head[:, i % HEADS, :]
                    if i >= HEADS:
                        act.wait_ge(tile_used, i - HEADS + 1)
                nc.scalar.copy(target, raw[:, q % RAW, :]).then_inc(head_ready, 1)
            act.wait_ge(eps_ready, 1)
            with act.Fori(0, G - 1) as g:
                for s in range(HALF, HALF + TILES):
                    if s == HALF + 3:
                        save_first(g)
                    if s == TILES + 6:
                        make_half_std(g)
                    make_head(g, s)
                store(g)
            for n, (s, j, blocks) in enumerate(PIECES):
                if (s, j) == (HALF + 2, 0):
                    save_first(G - 1)
                part = slice(j * W, (j + blocks) * W)
                act.wait_ge(piece_landed[n], 16)
                act.wait_ge(tile_used, TILES * (G - 1) + s - HEADS + 1)
                nc.scalar.copy(head[:, s % HEADS, part], raw[:, slot(s), part]).then_inc(head_ready, 1)
            act.wait_ge(tile_used, TILES * G)
            for part in range(2):
                cols = slice(part * W // 2, (part + 1) * W // 2)
                nc.scalar.copy(y_t[:, cols], acc[1][:, cols]).then_inc(last_y_ready, 1)
            for part in range(2):
                cols = slice(part * C // 2, (part + 1) * C // 2)
                act.wait_ge(var_ready, G + part)
                nc.scalar.activation(half_std[:, cols], mean_var[:, cols, 1], ACT.Sqrt, scale=0.25,
                                     bias=eps_quarter[:, :]).then_inc(half_std_ready, 1)

        @block.vector
        def _(dve):
            def make_rest(g, s):
                dve.wait_ge(raw_landed[slot(s)], landings(g, s))
                dve.wait_ge(head_ready, TILES * g + (X_TILES + s + 1))
                dve.wait_ge(tile_used, TILES * g + (s - RESTS + 1))
                nc.vector.tensor_tensor(rest[:, s % RESTS, :], raw[:, slot(s), :],
                                        head[:, s % HEADS, :].bitcast(fp32),
                                        ALU.subtract).then_inc(rest_ready, 1)

            def make_y_t(g):
                dve.wait_ge(tile_used, TILES * g + TILES)
                dve.wait_ge(first_saved, g + 1)
                nc.vector.tensor_tensor(y_t[:, :], acc[1][:, :], first_sum[:, :],
                                        ALU.add).then_inc(y_t_ready, 1)

            def gather_x(g):
                rows = bass.ds(g * W, W)
                nc.vector.tensor_tensor(residual[:, :], x_head[:, rows].bitcast(fp32),
                                        x_rest[:, rows].bitcast(fp32), ALU.add).then_inc(x_rows_ready, 1)

            def make_residual(g):
                dve.wait_ge(h_landed, 16 * g + 16)
                dve.wait_ge(x_rows_ready, g + 1)
                nc.vector.scalar_tensor_tensor(out=residual[:, :], in0=h_in[:, :], scalar=ALPHA,
                                               in1=residual[:, :], op0=ALU.mult,
                                               op1=ALU.add).then_inc(residual_ready, 1)

            def make_z(g):
                dve.wait_ge(turned_ready, g + 1)
                dve.wait_ge(residual_ready, g + 1)
                nc.vector.scalar_tensor_tensor(out=z[:, :, :].rearrange("p c f -> p (c f)"),
                                               in0=turned[:, :], scalar=1.0 - ALPHA,
                                               in1=residual[:, :], op0=ALU.mult,
                                               op1=ALU.add).then_inc(z_ready, 1)

            def make_stats(g):
                dve.wait_ge(z_ready, g + 1)
                for c in range(C):
                    nc.vector.bn_stats(stats[:, c, :], z[:, c, :]).then_inc(stats_ready, 1)

            def make_var(g):
                for c in range(C):
                    last = nc.vector.bn_aggr(mean_var[:, c, :], stats[:, c, :])
                last.then_inc(var_ready, 1)

            def make_rstd(n, cols):
                dve.wait_ge(half_std_ready, n + 1)
                nc.vector.reciprocal(inverse[:, cols], half_std[:, cols]).then_inc(std_steps, 1)
                dve.wait_ge(std_steps, 3 * n + 1)
                nc.vector.scalar_tensor_tensor(out=ratio[:, cols], in0=mean_var[:, cols, 1], scalar=EPS,
                                               in1=inverse[:, cols], op0=ALU.add,
                                               op1=ALU.mult).then_inc(std_steps, 1)
                dve.wait_ge(std_steps, 3 * n + 2)
                nc.vector.scalar_tensor_tensor(out=std[:, cols], in0=ratio[:, cols], scalar=0.25,
                                               in1=half_std[:, cols], op0=ALU.mult,
                                               op1=ALU.add).then_inc(std_steps, 1)
                dve.wait_ge(std_steps, 3 * n + 3)
                nc.vector.reciprocal(rstd[:, cols], std[:, cols]).then_inc(rstd_ready, 1)
                dve.wait_ge(rstd_ready, n + 1)

            def make_normed(g):
                make_rstd(g, slice(0, C))
                dve.wait_ge(normed_free, 16 * g + 16)
                for c in range(C):
                    last = nc.vector.tensor_scalar(normed[:, c, :], z[:, c, :], mean_var[:, c, 0:1],
                                                   rstd[:, c:c + 1], ALU.subtract, ALU.mult)
                last.then_inc(normed_ready, 1)

            for q, (what, i) in enumerate(LEAD_IN):
                dve.wait_ge(raw_landed[q % RAW], 16 * (q // RAW + 1))
                dve.wait_ge(head_ready, q + 1)
                if what == "x":
                    part = slice(i * TILE, (i + 1) * TILE)
                    target, its_head = x_rest[:, part], x_head[:, part]
                else:
                    target, its_head = rest[:, i % RESTS, :], head[:, i % HEADS, :]
                    if i >= RESTS:
                        dve.wait_ge(tile_used, i - RESTS + 1)
                nc.vector.tensor_tensor(target, raw[:, q % RAW, :], its_head.bitcast(fp32),
                                        ALU.subtract).then_inc(rest_ready, 1)
            with dve.Fori(0, G - 1) as g:
                for s in range(HALF, HALF + TILES):
                    if s == HALF + 2:
                        gather_x(g)
                    if s == HALF + 4:
                        make_residual(g)
                    if s == TILES + 1:
                        make_y_t(g)
                    if s == TILES + 3:
                        make_z(g)
                    if s == TILES + 4:
                        make_stats(g)
                        dve.wait_ge(stats_ready, C * g + C)
                    if s == TILES + 6:
                        make_normed(g)
                    make_rest(g, s)
                    if s == TILES + 4:
                        make_var(g)
            for n, (s, j, blocks) in enumerate(PIECES):
                if (s, j) == (HALF + 1, 0):
                    gather_x(G - 1)
                if (s, j) == (HALF + 2, 0):
                    make_residual(G - 1)
                if (s, j) == (HALF + 4, 0):
                    make_z(G - 1)
                part = slice(j * W, (j + blocks) * W)
                dve.wait_ge(piece_landed[n], 16)
                dve.wait_ge(head_ready, SPLITS + n + 1)
                dve.wait_ge(tile_used, TILES * (G - 1) + s - RESTS + 1)
                nc.vector.tensor_tensor(rest[:, s % RESTS, part], raw[:, slot(s), part],
                                        head[:, s % HEADS, part].bitcast(fp32),
                                        ALU.subtract).then_inc(rest_ready, 1)
            for part in range(2):
                blocks = range(part * C // 2, (part + 1) * C // 2)
                z_part = z[:, blocks.start:blocks.stop, :].rearrange("p c f -> p (c f)")
                dve.wait_ge(last_turned_ready, part + 1)
                dve.wait_ge(z_ready, G)
                nc.vector.scalar_tensor_tensor(out=z_part, in0=last_turned[part][:, 0:W // 2],
                                               scalar=1.0 - ALPHA, in1=z_part, op0=ALU.mult,
                                               op1=ALU.add).then_inc(last_z_ready, 1)
                dve.wait_ge(last_z_ready, part + 1)
                for c in blocks:
                    nc.vector.bn_stats(stats[:, c, :], z[:, c, :]).then_inc(stats_ready, 1)
                for c in blocks:
                    dve.wait_ge(stats_ready, C * (G - 1) + c + 1)
                    last = nc.vector.bn_aggr(mean_var[:, c, :], stats[:, c, :])
                last.then_inc(var_ready, 1)
            dve.wait_ge(normed_free, 16 * G)
            for part in range(2):
                blocks = range(part * C // 2, (part + 1) * C // 2)
                make_rstd(G - 1 + part, slice(blocks.start, blocks.stop))
                for c in blocks:
                    last = nc.vector.tensor_scalar(normed[:, c, :], z[:, c, :], mean_var[:, c, 0:1],
                                                   rstd[:, c:c + 1], ALU.subtract, ALU.mult)
                last.then_inc(normed_ready, 1)

        @block.tensor
        def _(pe):
            def multiply(g, s, ready):
                bank = acc[s // HALF % 2]
                place = s % HALF
                blocks = [slice(j * F, (j + 1) * F) for j in range(C * (s % TILES), C * (s % TILES) + C)]
                pe.wait_ge(head_ready, ready)
                for j, k in enumerate(blocks):
                    moving = head[:, s % HEADS, j * W:(j + 1) * W]
                    nc.tensor.matmul(bank[:, :], x_head[:, k], moving,
                                     start=(place == 0 and j == 0), stop=False)
                    nc.tensor.matmul(bank[:, :], x_rest[:, k], moving, start=False, stop=False)
                pe.wait_ge(rest_ready, ready)
                for j, k in enumerate(blocks):
                    last = nc.tensor.matmul(bank[:, :], x_head[:, k], rest[:, s % RESTS, j * W:(j + 1) * W],
                                            start=False, stop=(place == HALF - 1 and j == C - 1))
                last.then_inc(tile_used, 1)

            def turn_blocks(source):
                for c in range(C):
                    last = nc.tensor.transpose(turned[:, c * P:(c + 1) * P], source[:, c * P:(c + 1) * P],
                                               identity[:, :])
                last.then_inc(turned_ready, 1)

            def turn(g):
                pe.wait_ge(y_t_ready, g + 1)
                turn_blocks(y_t)

            pe.wait_ge(identity_ready, 1)
            for q, (what, i) in enumerate(LEAD_IN):
                if what == "x":
                    pe.wait_ge(head_ready, q + 1)
                    pe.wait_ge(rest_ready, q + 1)
                else:
                    multiply(0, i, q + 1)
            with pe.Fori(0, G - 1) as g:
                for s in range(HALF, HALF + TILES):
                    if s == TILES:
                        pe.wait_ge(first_saved, g + 1)
                    if s == TILES + 2:
                        turn(g)
                    multiply(g, s, TILES * g + (X_TILES + s + 1))
            for n in range(len(PIECES) + 1):
                if n < len(PIECES):
                    s, first, blocks = PIECES[n]
                    if (s, first) == (HALF + 3, 0):
                        pe.wait_ge(first_saved, G)
                        turn_blocks(first_sum)
                    pe.wait_ge(head_ready, SPLITS + n + 1)
                    for j in range(first, first + blocks):
                        k = slice((C * s + j) * F, (C * s + j + 1) * F)
                        cols = slice(j * W, (j + 1) * W)
                        nc.tensor.matmul(acc[1][:, :], x_head[:, k], head[:, s % HEADS, cols],
                                         start=(n == 0 and j == 0), stop=False)
                        nc.tensor.matmul(acc[1][:, :], x_rest[:, k], head[:, s % HEADS, cols],
                                         start=False, stop=False)
                if n > 0:
                    s, first, blocks = PIECES[n - 1]
                    pe.wait_ge(rest_ready, SPLITS + n)
                    for j in range(first, first + blocks):
                        k = slice((C * s + j) * F, (C * s + j + 1) * F)
                        cols = slice(j * W, (j + 1) * W)
                        last = nc.tensor.matmul(acc[1][:, :], x_head[:, k], rest[:, s % RESTS, cols],
                                                start=False, stop=(n == len(PIECES) and j == C - 1))
                    if first + blocks == C:
                        last.then_inc(tile_used, 1)
            for part in range(2):
                pe.wait_ge(last_y_ready, part + 1)
                for c in range(C // 2):
                    at = part * W // 2 + c * P
                    last = nc.tensor.transpose(last_turned[part][:, c * P:(c + 1) * P],
                                               y_t[:, at:at + P], identity[:, :])
                last.then_inc(last_turned_ready, 1)


def kernel(x, adj, L0_gnn_h):
    import concourse.bacc as bacc
    from concourse.bass_utils import run_bass_kernel_spmd

    x, adj, h = (np.asarray(a) for a in (x, adj, L0_gnn_h))
    arrays = {
        "x": np.ascontiguousarray(x.reshape(G, P, C * F).transpose(1, 0, 2).reshape(P, -1)),
        "adj": np.ascontiguousarray(
            adj.reshape(G, P, C, G, P, C).transpose(0, 3, 4, 5, 2, 1).reshape(G * TILES, P, TILE)),
        "h": np.ascontiguousarray(h.reshape(G, P, C * F)),
    }
    nc = bacc.Bacc("TRN2", target_bir_lowering=False, num_devices=1)
    fp32 = mybir.dt.float32
    args = [nc.dram_tensor(name, a.shape, fp32, kind="ExternalInput").ap() for name, a in arrays.items()]
    out = nc.dram_tensor("out", (G, P, C * F), fp32, kind="ExternalOutput").ap()
    build(nc, *args, out)
    result = run_bass_kernel_spmd(nc, [arrays], core_ids=[0]).results[0]["out"]
    return result.reshape(N, F)
```
